# Optimizing a Trainium2 kernel written in Bass

```python
import numpy as np
import jax
import jax.numpy as jnp

def _softmax(x, axis=-1):
    return jax.nn.softmax(x, axis=axis)

def _gelu(x):
    return jax.nn.gelu(x, approximate=True)

def _silu(x):
    return jax.nn.silu(x)

def _sigmoid(x):
    return jax.nn.sigmoid(x)

def _layernorm(x, axis=-1, eps=1e-05):
    m = jnp.mean(x, axis=axis, keepdims=True)
    v = jnp.var(x, axis=axis, keepdims=True)
    return (x - m) / jnp.sqrt(v + eps)

def _scatter_add(tgt, idx, src, axis=0):
    return tgt.at[idx].add(src)

def _segment_sum(src, seg, n):
    return jax.ops.segment_sum(src, seg, n)
kernel_name = 'mk_adj_resnorm_d2_adj_r2_75b2b4'

def setup_inputs(seed: int=0):
    np.random.seed(seed)
    _w = jnp.asarray

    def _rec_inputs():
        import jax
        import jax.numpy as jnp
        _gk = jax.random.key(seed)
        x = -0.0002928 + 1 * jax.random.normal(jax.random.fold_in(_gk, 1), (4096, 256), jnp.float32)
        _a = jax.random.bernoulli(jax.random.fold_in(_gk, 2), 0.00195312, (4096, 4096))
        adj = _a.astype(jnp.int32)
        return (x, adj)
    x, adj = _rec_inputs()

    def _L0_gnn_setup():
        import jax, jax.numpy as jnp
        import numpy as np
        N, D_IN, D_OUT = (4096, 256, 256)
        key = jax.random.key(seed)
        ks = jax.random.split(key, 8)
        scale_in = 1.0 / np.sqrt(D_IN)
        scale_cat = 1.0 / np.sqrt(2 * D_OUT)
        return {'x': jax.random.normal(ks[0], (N, D_IN), dtype=jnp.float32), 'adj': jax.random.randint(ks[1], (N, N), 0, 2, dtype=jnp.int32), 'W_self': jax.random.uniform(ks[2], (D_IN, D_OUT), jnp.float32, -scale_in, scale_in), 'b_self': jax.random.uniform(ks[3], (D_OUT,), jnp.float32, -scale_in, scale_in), 'W_nb': jax.random.uniform(ks[4], (D_IN, D_OUT), jnp.float32, -scale_in, scale_in), 'b_nb': jax.random.uniform(ks[5], (D_OUT,), jnp.float32, -scale_in, scale_in), 'W_comb': jax.random.uniform(ks[6], (2 * D_OUT, D_OUT), jnp.float32, -scale_cat, scale_cat), 'b_comb': jax.random.uniform(ks[7], (D_OUT,), jnp.float32, -scale_cat, scale_cat)}
    _L0_gnn_all = _L0_gnn_setup()
    _L0_gnn_in = {k: v for k, v in _L0_gnn_all.items() if k in ('W_self', 'b_self', 'W_nb', 'b_nb', 'W_comb', 'b_comb')}
    del _L0_gnn_all

    def _L1_gnn_setup():
        import jax, jax.numpy as jnp
        import numpy as np
        N_X, N_NEIGH, D_IN, D_HID, D_OUT = (4096, 4096, 256, 32, 128)
        NEG_BIG = -9000000000000000.0
        key = jax.random.key(seed)
        ks = jax.random.split(key, 16)
        s_in = 1.0 / np.sqrt(D_IN)
        s_hid = 1.0 / np.sqrt(D_HID)
        return {'x': jax.random.normal(ks[0], (N_X, D_IN), jnp.float32), 'neigh': jax.random.normal(ks[1], (N_NEIGH, D_IN), jnp.float32), 'adj': jax.random.randint(ks[2], (N_X, N_NEIGH), 0, 2, jnp.int32), 'Wx1': jax.random.uniform(ks[3], (D_IN, D_HID), jnp.float32, -s_in, s_in), 'bx1': jnp.zeros((D_HID,), jnp.float32), 'Wx2': jax.random.uniform(ks[4], (D_HID, D_HID), jnp.float32, -s_hid, s_hid), 'bx2': jnp.zeros((D_HID,), jnp.float32), 'Wn1': jax.random.uniform(ks[5], (D_IN, D_HID), jnp.float32, -s_in, s_in), 'bn1': jnp.zeros((D_HID,), jnp.float32), 'Wn2': jax.random.uniform(ks[6], (D_HID, D_HID), jnp.float32, -s_hid, s_hid), 'bn2': jnp.zeros((D_HID,), jnp.float32), 'Wv': jax.random.uniform(ks[7], (D_IN, D_OUT), jnp.float32, -s_in, s_in), 'bv': jnp.zeros((D_OUT,), jnp.float32), 'Wfx': jax.random.uniform(ks[8], (D_IN, D_OUT), jnp.float32, -s_in, s_in), 'bfx': jnp.zeros((D_OUT,), jnp.float32)}
    _L1_gnn_all = _L1_gnn_setup()
    _L1_gnn_in = {k: v for k, v in _L1_gnn_all.items() if k in ('neigh', 'Wx1', 'bx1', 'Wx2', 'bx2', 'Wn1', 'bn1', 'Wn2', 'bn2', 'Wv', 'bv', 'Wfx', 'bfx')}
    del _L1_gnn_all
    return {'x': x, 'adj': adj, 'L0_gnn_W_self': _L0_gnn_in['W_self'], 'L0_gnn_b_self': _L0_gnn_in['b_self'], 'L0_gnn_W_nb': _L0_gnn_in['W_nb'], 'L0_gnn_b_nb': _L0_gnn_in['b_nb'], 'L0_gnn_W_comb': _L0_gnn_in['W_comb'], 'L0_gnn_b_comb': _L0_gnn_in['b_comb'], 'L1_gnn_neigh': _L1_gnn_in['neigh'], 'L1_gnn_Wx1': _L1_gnn_in['Wx1'], 'L1_gnn_bx1': _L1_gnn_in['bx1'], 'L1_gnn_Wx2': _L1_gnn_in['Wx2'], 'L1_gnn_bx2': _L1_gnn_in['bx2'], 'L1_gnn_Wn1': _L1_gnn_in['Wn1'], 'L1_gnn_bn1': _L1_gnn_in['bn1'], 'L1_gnn_Wn2': _L1_gnn_in['Wn2'], 'L1_gnn_bn2': _L1_gnn_in['bn2'], 'L1_gnn_Wv': _L1_gnn_in['Wv'], 'L1_gnn_bv': _L1_gnn_in['bv'], 'L1_gnn_Wfx': _L1_gnn_in['Wfx'], 'L1_gnn_bfx': _L1_gnn_in['bfx']}

def reference(x, adj, L0_gnn_W_self, L0_gnn_b_self, L0_gnn_W_nb, L0_gnn_b_nb, L0_gnn_W_comb, L0_gnn_b_comb, L1_gnn_neigh, L1_gnn_Wx1, L1_gnn_bx1, L1_gnn_Wx2, L1_gnn_bx2, L1_gnn_Wn1, L1_gnn_bn1, L1_gnn_Wn2, L1_gnn_bn2, L1_gnn_Wv, L1_gnn_bv, L1_gnn_Wfx, L1_gnn_bfx):
    import jax
    import jax.numpy as jnp

    def _L0_gnn_ref(x, adj, W_self, b_self, W_nb, b_nb, W_comb, b_comb):
        import jax, jax.numpy as jnp
        import numpy as np
        N, D_IN, D_OUT = (4096, 256, 256)
        mask = (adj > 0).astype(x.dtype)
        deg = jnp.sum(mask, axis=1, keepdims=True)
        agg = mask @ x / jnp.maximum(deg, 1.0)
        self_f = x @ W_self + b_self
        nb_f = agg @ W_nb + b_nb
        combined = jnp.concatenate([self_f, nb_f], axis=-1)
        out = combined @ W_comb + b_comb
        return jax.nn.relu(out)

    def _L1_gnn_ref(x, neigh, adj, Wx1, bx1, Wx2, bx2, Wn1, bn1, Wn2, bn2, Wv, bv, Wfx, bfx):
        import jax, jax.numpy as jnp
        import numpy as np
        N_X, N_NEIGH, D_IN, D_HID, D_OUT = (4096, 4096, 256, 32, 128)
        NEG_BIG = -9000000000000000.0
        neib_att = jnp.tanh(neigh @ Wn1 + bn1) @ Wn2 + bn2
        value = neigh @ Wv + bv
        x_att = jnp.tanh(x @ Wx1 + bx1) @ Wx2 + bx2
        ws = jnp.einsum('nh,mh->nm', x_att, neib_att)
        ws = jax.nn.leaky_relu(ws, negative_slope=0.01)
        ws = jnp.where(adj > 0, ws, jnp.float32(NEG_BIG))
        ws = jax.nn.softmax(ws, axis=1)
        agg_neib = ws @ value
        out = jnp.concatenate([x @ Wfx + bfx, agg_neib], axis=1)
        return out
    x = _layernorm(x + _L0_gnn_ref(x, adj, L0_gnn_W_self, L0_gnn_b_self, L0_gnn_W_nb, L0_gnn_b_nb, L0_gnn_W_comb, L0_gnn_b_comb), axis=-1)
    x = _layernorm(x + _L1_gnn_ref(x, L1_gnn_neigh, adj, L1_gnn_Wx1, L1_gnn_bx1, L1_gnn_Wx2, L1_gnn_bx2, L1_gnn_Wn1, L1_gnn_bn1, L1_gnn_Wn2, L1_gnn_bn2, L1_gnn_Wv, L1_gnn_bv, L1_gnn_Wfx, L1_gnn_bfx), axis=-1)
    return x

_drawn_inputs = setup_inputs


def setup_inputs(seed=0):
    import zlib

    import numpy as np

    out = dict(_drawn_inputs(seed))
    spreads = {'L1_gnn_bx1': (0.0, 2.0),
     'L1_gnn_bx2': (0.0, 0.649),
     'L1_gnn_bn1': (0.0, 2.0),
     'L1_gnn_bn2': (0.0, 0.8),
     'L1_gnn_bv': (0.0, 0.1),
     'L1_gnn_bfx': (0.0, 0.1)}
    factors = {'L0_gnn_b_self': 6.303,
     'L0_gnn_b_nb': 5.179,
     'L0_gnn_b_comb': 3.139,
     'L1_gnn_Wx1': 8.0,
     'L1_gnn_Wx2': 8.0,
     'L1_gnn_Wn1': 8.0,
     'L1_gnn_Wn2': 5.235}
    for name, (base, spread) in spreads.items():
        noise = np.random.default_rng([zlib.crc32(name.encode()), seed]).standard_normal(out[name].shape)
        drawn = base * np.exp(spread * noise) if base else spread * noise
        out[name] = jnp.asarray(drawn.astype(out[name].dtype))
    for name, factor in factors.items():
        out[name] = (out[name] * factor).astype(out[name].dtype)
    return out
```

```python
from contextlib import ExitStack

import concourse.bass as bass
from concourse import mybir

F32, F16, BF16 = mybir.dt.float32, mybir.dt.float16, mybir.dt.bfloat16
I32, U32 = mybir.dt.int32, mybir.dt.uint32
ALU = mybir.AluOpType
ACT = mybir.ActivationFunctionType
AX = mybir.AxisListType
RMAX = bass.bass_isa.ReduceOp.max

P = 128
N = 4096
D = 256
H = 32
DV = 128
NB = N // P
NC = N // P
DC = D // P
QW = 1024
NQ = N // QW
GW = 512
NG = N // GW
CQ = QW // P
CG = GW // P
YW = 2 * D + 2
Y_ONE, Y_LO = D, D + 2
BIG = 2.0 ** 100
SLOPE = 0.01
LN_EPS = 1e-5
EXP_SHIFT = 14 * 0.6931471805599453
TOP = 2.0 ** 13
TINY = 2.0 ** -100
PROLOGUE_ROWS = 4
PT = NB // PROLOGUE_ROWS


class Block:

    def __init__(self, i, off, end=NB):
        self.i, self.off, self.end = i, off, end
        self.n = off if i is None else 2 * i + off
        self.odd = off % 2
        self.pair = off // 2 if i is None else i + off // 2
        self.exists = i is not None or 0 <= off < end

    def plus(self, k):
        return Block(self.i, self.off + k, self.end)

    def is_first(self):
        return self.i is None and self.off == 0


def walk(eng, step):
    for t in (-2, -1, 0, 1, 2):
        step(Block(None, t))
    with eng.Fori(0, (NB - 6) // 2) as i:
        step(Block(i, 3))
        step(Block(i, 4))
    for t in range(NB - 3, NB + 2):
        step(Block(None, t))


def turns(eng, step):
    step(Block(None, 0, PT))
    step(Block(None, 1, PT))
    with eng.Fori(0, (PT - 4) // 2) as i:
        step(Block(i, 2, PT))
        step(Block(i, 3, PT))
    step(Block(None, PT - 2, PT))
    step(Block(None, PT - 1, PT))


def at_least(eng, sem, value):
    if isinstance(value, int) and value <= 0:
        return
    eng.wait_ge(sem, value)


def apart(eng, passed):
    eng.sem_inc(passed, 1)


def gnn_kernel(nc, x, adj, w_self, b_self, w_nb, b_nb, w_comb, b_comb, neigh, wx1, bx1, wx2, bx2,
               wn1, bn1, wn2, bn2, wv, bv, wfx, bfx, out):
    x_blocks = x.rearrange("(b p) d -> b p d", p=P)
    out_blocks = out.rearrange("(b p) d -> b p d", p=P)
    adj_blocks = adj.rearrange("(b p) (q w) -> b q p w", p=P, w=QW)

    with ExitStack() as ctx:
        def sb(name, shape, dt):
            return ctx.enter_context(nc.sbuf_tensor(name, shape, dt))

        def sem(name):
            return ctx.enter_context(nc.semaphore(name))

        y16 = sb("y16", [P, NC, YW], F16)
        z = sb("z", [P, NB, D], F32)
        v16 = sb("v16", [P, NC, 2 * DV], F16)
        n16 = sb("n16", [P, N], F16)
        ident = sb("ident", [P, P], F32)
        wfx_sb = sb("wfx_sb", [P, DC, DV], F32)
        wx1_sb = sb("wx1_sb", [P, DC, H], F32)
        wx2_sb = sb("wx2_sb", [H, 4 * H], F32)
        bx1_sb = sb("bx1_sb", [H, 1], F32)
        bx2_sb = sb("bx2_sb", [P, 1], F32)
        bfx_sb = sb("bfx_sb", [P, D], F32)
        sc = sb("sc", [P, 16], F32)
        g_wb, p_xn, s_xn, score_scale, y_top, y_scale, y_inv, v_top, v_scale, v_inv = (
            sc[:, 0:4], sc[:, 4:6], sc[:, 6:8], sc[:, 8:9], sc[:, 9:10], sc[:, 10:11], sc[:, 11:12],
            sc[:, 12:13], sc[:, 13:14], sc[:, 14:15])
        minus_half = sb("minus_half", [P, 1], F32)

        adj_sb = sb("adj_sb", [P, NQ, QW], I32)
        bias = sb("bias", [P, 2, N], BF16)
        mask = sb("mask", [P, N], BF16)
        mask_t = sb("mask_t", [P, NC, P], BF16)
        score = sb("score", [P, 2, N], F32)
        bend = sb("bend", [P, 2, QW], F32)
        p_hi = sb("p_hi", [P, 2, GW], F16)
        p_lo = sb("p_lo", [P, 2, GW], F16)
        x_in = sb("x_in", [P, 2, D], F32)
        l0 = sb("l0", [P, D], F32)
        x1 = sb("x1", [P, D], F32)
        x1_t = sb("x1_t", [P, D], F32)
        tanh_sb = sb("tanh_sb", [H, P], F32)
        stack = sb("stack", [P, P], F16)
        res = sb("res", [P, 2, D], F32)
        out_sb = sb("out_sb", [P, D], F32)
        part_max = sb("part_max", [P, NG], F32)
        row = sb("row", [P, 8], F32)
        sums = sb("sums", [P, 2, NQ], F32)
        row2 = sb("row2", [P, 4], F32)
        stat1 = sb("stat1", [P, 6], F32)
        mv1 = sb("mv1", [P, 4], F32)
        stat2 = sb("stat2", [P, 6], F32)
        mv2 = sb("mv2", [P, 4], F32)

        wvn = sb("wvn", [P, DC, DV + H], F32)
        bvn = sb("bvn", [P, DV + H], F32)
        wn2_sb = sb("wn2_sb", [H, 4 * H], F32)
        bn2_sb = sb("bn2_sb", [P, 1], F32)
        z_bias = sb("z_bias", [P, D], F32)
        b_cols = sb("b_cols", [P, 2 * DC], F32)
        v_tops = sb("v_tops", [P, PT], F32)
        y_tops = sb("y_tops", [P, NB], F32)
        h_row = sb("h_row", [P, 2, PROLOGUE_ROWS, H], F32)
        raw = score[:, 0, :]
        ws_raw = raw[:, 0:512].rearrange("p (c n) -> p c n", c=DC)
        wn_raw = raw[:, 512:1024].rearrange("p (c n) -> p c n", c=DC)
        wc_raw = raw[:, 1024:2048].rearrange("p (c n) -> p c n", c=2 * DC)
        ws_t, wn_t = raw[:, 2048:2560], raw[:, 2560:3072]
        b_wide = raw[:, 3072:3584].rearrange("p (c n) -> p c n", c=2 * DC)
        y32 = score[:, :, :].rearrange("p a n -> p (a n)").rearrange("p (b d) -> p b d", d=D)
        v32 = bias[:, :, :].rearrange("p a n -> p (a n)").bitcast(F32).rearrange("p (b d) -> p b d", d=DV)
        row_in = mask_t[:, :, :].rearrange("p c n -> p (c n)").bitcast(F32).rearrange(
            "p (s b d) -> p s b d", s=2, d=D)
        rows_t = bend[:, :, :].rearrange("p a n -> p (a n)").rearrange("p (s c n) -> p s c n", s=2, c=DC)
        m_both = mask[:, :].bitcast(F32)[:, 0:1024].rearrange("p (c n) -> p c n", c=DC)
        h_t = mask[:, :].bitcast(F32)[0:H, 1024:1536]

        ps_agg = [ctx.enter_context(nc.psum_tensor(f"ps_agg{k}", [P, GW], F32)) for k in range(2)]
        ps_s = [ctx.enter_context(nc.psum_tensor(f"ps_s{k}", [P, GW], F32)) for k in range(2)]
        ps_t = [ctx.enter_context(nc.psum_tensor(f"ps_t{k}", [P, GW], F32)) for k in range(2)]
        ps_v = ctx.enter_context(nc.psum_tensor("ps_v", [P, GW], F32))
        ps_x = ctx.enter_context(nc.psum_tensor("ps_x", [P, GW], F32))

        weights_in = sem("weights_in")
        rows_in = [sem(f"rows_in{k}") for k in range(2)]
        adj_in = [sem(f"adj_in{q}") for q in range(NQ)]
        mask_t_in = [sem(f"mask_t_in{q}") for q in range(NQ)]
        x_in_in = [sem(f"x_in_in{k}") for k in range(2)]
        out_sent = sem("out_sent")
        dve_passed = sem("dve_passed")
        sp_passed = sem("sp_passed")
        ident_ready = sem("ident_ready")
        consts_ready = sem("consts_ready")
        w_transposed = sem("w_transposed")
        w_t_copied = sem("w_t_copied")
        b_wide_made = sem("b_wide_made")
        m_done = sem("m_done")
        m_copied = sem("m_copied")
        bound_made = sem("bound_made")
        bound_reduced = sem("bound_reduced")
        scale_step = sem("scale_step")
        bounds_scaled = sem("bounds_scaled")
        v_scaled = sem("v_scaled")
        y_scaled = sem("y_scaled")
        rows_transposed = sem("rows_transposed")
        rows_t_act = sem("rows_t_act")
        rows_t_dve = sem("rows_t_dve")
        vh_done = sem("vh_done")
        vh_read = sem("vh_read")
        h_made = sem("h_made")
        h_tanh = sem("h_tanh")
        h_transposed = sem("h_transposed")
        h_t_copied = sem("h_t_copied")
        natt_done = sem("natt_done")
        natt_hi = sem("natt_hi")
        natt_lo = sem("natt_lo")
        v_top_made = sem("v_top_made")
        v_top_reduced = sem("v_top_reduced")
        v_hi_made = sem("v_hi_made")
        v_lo_made = sem("v_lo_made")
        yz_done = sem("yz_done")
        y_copied = sem("y_copied")
        yz_read = sem("yz_read")
        y_top_made = sem("y_top_made")
        y_top_reduced = sem("y_top_reduced")
        y_hi_made = sem("y_hi_made")
        y_lo_made = sem("y_lo_made")
        agg_done = sem("agg_done")
        s_done = sem("s_done")
        pt_done = sem("pt_done")
        pv_done = sem("pv_done")
        x1_t_done = sem("x1_t_done")
        hf_done = sem("hf_done")
        xatt_done = sem("xatt_done")
        bias_made = sem("bias_made")
        mask_made_dve = sem("mask_made_dve")
        score_made = sem("score_made")
        max_step = sem("max_step")
        l0_step = sem("l0_step")
        agg_read = sem("agg_read")
        x1_made = sem("x1_made")
        stack_ready = sem("stack_ready")
        p_lo_made = sem("p_lo_made")
        res_made = sem("res_made")
        l1_step = sem("l1_step")
        out_made = sem("out_made")
        mask_made_act = sem("mask_made_act")
        bend_made = sem("bend_made")
        exp_made = sem("exp_made")
        p_hi_made = sem("p_hi_made")
        x1_t_copied = sem("x1_t_copied")
        tanh_made = sem("tanh_made")
        xatt_hi = sem("xatt_hi")
        leaky_made = sem("leaky_made")
        rstd1_made = sem("rstd1_made")
        rstd2_made = sem("rstd2_made")
        resx_made = sem("resx_made")

        SMALL_DMAS = [
            (ws_raw, w_self.rearrange("(c p) n -> p c n", p=P)),
            (wn_raw, w_nb.rearrange("(c p) n -> p c n", p=P)),
            (wc_raw, w_comb.rearrange("(c p) n -> p c n", p=P)),
            (z_bias[:, :], b_comb.partition_broadcast(P)),
            (wvn[:, :, 0:DV], wv.rearrange("(c p) n -> p c n", p=P)),
            (wvn[:, :, DV:DV + H], wn1.rearrange("(c p) n -> p c n", p=P)),
            (bvn[:, 0:DV], bv.partition_broadcast(P)),
            (bvn[:, DV:DV + H], bn1.partition_broadcast(P)),
            (wfx_sb[:, :, :], wfx.rearrange("(c p) n -> p c n", p=P)),
            (wx1_sb[:, :, :], wx1.rearrange("(c p) n -> p c n", p=P)),
            (bx1_sb[:, :], bx1.rearrange("(h o) -> h o", o=1)),
            (bfx_sb[:, 0:DV], bfx.partition_broadcast(P)),
        ] + [(b_cols[:, k * DC + c:k * DC + c + 1], b.rearrange("(c p o) -> c p o", p=P, o=1)[c])
             for k, b in enumerate((b_self, b_nb)) for c in range(DC)] \
          + [(wx2_sb[:, k * H:(k + 1) * H], wx2) for k in range(4)] \
          + [(wn2_sb[:, k * H:(k + 1) * H], wn2) for k in range(4)] \
          + [(bx2_sb[k * H:(k + 1) * H, :], bx2.rearrange("(h o) -> h o", o=1)) for k in range(4)] \
          + [(bn2_sb[k * H:(k + 1) * H, :], bn2.rearrange("(h o) -> h o", o=1)) for k in range(4)]

        block = ctx.enter_context(nc.Block())

        @block.sync
        def _(sp):
            def wait(sem, value):
                at_least(sp, sem, value)
                if not isinstance(value, int):
                    apart(sp, sp_passed)

            def load_rows(source, turn, first):
                wait(rows_transposed, 2 * (turn.n + first) - 2)
                sp.dma_start(row_in[:, turn.odd],
                             source[bass.ds(PROLOGUE_ROWS * P * turn.n, PROLOGUE_ROWS * P), :].rearrange(
                                 "(b p) d -> p b d", p=P)).then_inc(rows_in[turn.odd], 16)

            for dst, src in SMALL_DMAS:
                sp.dma_start(dst, src).then_inc(weights_in, 16)
            turns(sp, lambda turn: load_rows(neigh, turn, 0))
            turns(sp, lambda turn: load_rows(x, turn, PT))

            def step(t):
                ahead, load, done = t.plus(2), t.plus(3), t.plus(-2)
                if t.off == -2 and t.i is None:
                    for q in range(NQ):
                        sp.dma_start(adj_sb[:, q, :], adj_blocks[0, q]).then_inc(adj_in[q], 16)
                if ahead.exists:
                    wait(l0_step, 9 * (ahead.n - 2) + 6)
                    sp.dma_start(x_in[:, ahead.odd, :], x_blocks[ahead.n]).then_inc(x_in_in[ahead.odd], 16)
                for q in range(NQ):
                    if ahead.exists:
                        if q < 2:
                            wait(mask_made_dve, 2 * ahead.n + q + 1)
                        else:
                            wait(mask_made_act, 2 * ahead.n + q - 1)
                        if ahead.is_first():
                            sp.wait_ge(rows_transposed, 4 * PT)
                        wait(agg_done, NQ * (ahead.n - 1) + q + 1)
                        sp.dma_start_transpose(mask_t[:, q * CQ:(q + 1) * CQ, :],
                                               mask[:, q * QW:(q + 1) * QW]).then_inc(mask_t_in[q], 16)
                    if load.exists and ahead.exists:
                        wait(bias_made, NQ * ahead.n + q + 1)
                        sp.dma_start(adj_sb[:, q, :], adj_blocks[load.n, q]).then_inc(adj_in[q], 16)
                if done.exists:
                    wait(out_made, done.n + 1)
                    sp.dma_start(out_blocks[done.n], out_sb[:, :]).then_inc(out_sent, 16)

            walk(sp, step)
            sp.wait_ge(out_sent, 16 * NB)

        @block.gpsimd
        def _(pool):
            pool.memset(ident[:, :], 0.0).then_inc(consts_ready, 1)
            pool.memset(minus_half[:, :], -0.5).then_inc(consts_ready, 1)
            pool.memset(sc[:, :], 0.0).then_inc(consts_ready, 1)
            pool.memset(bfx_sb[:, DV:D], 0.0).then_inc(consts_ready, 1)
            pool.memset(y16[:, :, Y_ONE:Y_LO], 1.0).then_inc(consts_ready, 1)
            pool.wait_ge(consts_ready, 1)
            pool.affine_select(out=ident[:, :], in_=ident[:, :], compare_op=ALU.not_equal, fill=1.0, base=0,
                               pattern=[[-1, P]], channel_multiplier=1).then_inc(ident_ready, 1)
            pool.wait_ge(bound_made, 4)
            pool.partition_all_reduce(g_wb, g_wb, P, RMAX).then_inc(bound_reduced, 1)
            pool.wait_ge(v_top_made, PT + 1)
            pool.partition_all_reduce(v_top, v_top, P, RMAX).then_inc(v_top_reduced, 1)
            pool.wait_ge(y_top_made, NB + 1)
            pool.partition_all_reduce(y_top, y_top, P, RMAX).then_inc(y_top_reduced, 1)

            def add_bend(t, q):
                pool.wait_ge(bend_made, NQ * t.n + q + 1)
                part = score[:, t.odd, q * QW:(q + 1) * QW]
                pool.tensor_tensor(part, part, bend[:, q % 2, :], ALU.add).then_inc(leaky_made, 1)

            def step(t):
                enter, done = t.plus(1), t.plus(-2)
                if t.exists:
                    add_bend(t, 0)
                if done.exists:
                    pool.wait_ge(l1_step, 7 * done.n + 7)
                    pool.tensor_tensor(mv2[:, 3:4], mv2[:, 2:3], minus_half[:, :], ALU.pow).then_inc(rstd2_made, 1)
                if t.exists:
                    add_bend(t, 1)
                    add_bend(t, 2)
                    pool.wait_ge(x1_made, t.n + 1)
                    at_least(pool, out_made, t.n - 1)
                    pool.tensor_tensor(res[:, t.odd, :], x1[:, :], bfx_sb[:, :], ALU.add).then_inc(resx_made, 1)
                if enter.exists:
                    pool.wait_ge(l0_step, 9 * enter.n + 9)
                    pool.tensor_tensor(mv1[:, 3:4], mv1[:, 2:3], minus_half[:, :], ALU.pow).then_inc(rstd1_made, 1)
                if t.exists:
                    add_bend(t, 3)

            walk(pool, step)

        @block.vector
        def _(dve):
            scale_count = [0]

            def scale_link(ins):
                ins.then_inc(scale_step, 1)
                scale_count[0] += 1
                dve.wait_ge(scale_step, scale_count[0])

            def power_below(dst, src):
                scale_link(dve.tensor_scalar(dst, src, TINY, None, ALU.max))
                scale_link(dve.tensor_scalar(dst.bitcast(U32), dst.bitcast(U32), 0x7F800000, None, ALU.bitwise_and))

            dve.wait_ge(weights_in, 16 * len(SMALL_DMAS))
            dve.wait_ge(consts_ready, 5)
            for k, w in enumerate((wx2_sb, bx2_sb, wn2_sb, bn2_sb)):
                n = H if k % 2 == 0 else P
                dve.tensor_reduce(sc[0:n, k:k + 1], w[:, :], AX.X, ALU.max,
                                  apply_absolute_value=True).then_inc(bound_made, 1)
            dve.wait_ge(ident_ready, 1)
            for c in range(2 * DC):
                dve.tensor_scalar(b_wide[:, c, :], ident[:, :], 0.0, b_cols[:, c:c + 1],
                                  ALU.mult, ALU.add).then_inc(b_wide_made, 1)
            dve.wait_ge(w_transposed, 1)
            dve.tensor_copy(ws_t, ps_t[0][:, :]).then_inc(w_t_copied, 1)
            dve.wait_ge(w_transposed, 2)
            dve.tensor_copy(wn_t, ps_t[1][:, :]).then_inc(w_t_copied, 1)
            dve.wait_ge(bound_reduced, 1)
            for k in range(2):
                scale_link(dve.tensor_scalar(p_xn[:, k:k + 1], sc[:, 2 * k:2 * k + 1], float(H),
                                             sc[:, 2 * k + 1:2 * k + 2], ALU.mult, ALU.add))
            power_below(p_xn, p_xn)
            scale_link(dve.reciprocal(s_xn, p_xn))
            scale_link(dve.tensor_scalar(s_xn, s_xn, TOP, None, ALU.mult))
            scale_link(dve.tensor_scalar(score_scale, p_xn[:, 0:1], p_xn[:, 1:2], SLOPE / TOP / TOP,
                                         ALU.mult, ALU.mult))
            scale_link(dve.tensor_scalar(wx2_sb[:, :], wx2_sb[:, :], s_xn[0:H, 0:1], None, ALU.mult))
            scale_link(dve.tensor_scalar(bx2_sb[:, :], bx2_sb[:, :], s_xn[:, 0:1], None, ALU.mult))
            scale_link(dve.tensor_scalar(wn2_sb[:, :], wn2_sb[:, :], s_xn[0:H, 1:2], None, ALU.mult))
            dve.tensor_scalar(bn2_sb[:, :], bn2_sb[:, :], s_xn[:, 1:2], None, ALU.mult).then_inc(bounds_scaled, 1)
            dve.wait_ge(bounds_scaled, 1)
            for c in range(DC):
                dve.wait_ge(m_done, c + 1)
                dve.tensor_copy(m_both[:, c, :], ps_s[c][:, :]).then_inc(m_copied, 1)
            dve.wait_ge(m_done, DC + 1)
            dve.tensor_tensor(z_bias[:, :], ps_v[:, 0:D], z_bias[:, :], ALU.add).then_inc(m_copied, 1)

            def copy_rows_t(turn, first, done):
                dve.wait_ge(rows_transposed, 2 * (turn.n + first) + 2)
                at_least(dve, done, PROLOGUE_ROWS * (turn.n - 1))
                dve.tensor_copy(rows_t[:, turn.odd, 1, :], ps_t[1][:, :]).then_inc(rows_t_dve, 1)

            def n_low(turn):
                dve.wait_ge(natt_hi, turn.n + 1)
                for s in (H, 3 * H):
                    part = n16[s:s + H, bass.ds(GW * turn.n, GW)]
                    ins = dve.scalar_tensor_tensor(out=part, in0=ps_agg[1][s:s + H, :], scalar=bn2_sb[s:s + H, 0:1],
                                                   in1=part, op0=ALU.add, op1=ALU.subtract)
                ins.then_inc(natt_lo, 1)

            def neigh_turn(turn):
                if turn.plus(1).exists:
                    copy_rows_t(turn.plus(1), 0, vh_done)
                first = PROLOGUE_ROWS * turn.n
                for u in range(PROLOGUE_ROWS):
                    dve.wait_ge(vh_done, first + u + 1)
                    if u == 0:
                        at_least(dve, h_transposed, turn.n - 1)
                    dve.tensor_tensor(h_row[:, turn.odd, u, :], ps_s[u % 2][:, DV:DV + H], bvn[:, DV:DV + H],
                                      ALU.add).then_inc(h_made, 1)
                    dve.tensor_tensor(v32[:, bass.ds(first + u, 1), :], ps_s[u % 2][:, 0:DV].unsqueeze(1),
                                      bvn[:, 0:DV].unsqueeze(1), ALU.add).then_inc(vh_read, 1)
                dve.wait_ge(vh_read, first + PROLOGUE_ROWS)
                dve.tensor_reduce(v_tops[:, bass.ds(turn.n, 1)], v32[:, bass.ds(first, PROLOGUE_ROWS), :],
                                  AX.XY, ALU.max, apply_absolute_value=True).then_inc(v_top_made, 1)
                if turn.plus(-1).exists:
                    n_low(turn.plus(-1))

            copy_rows_t(Block(None, 0), 0, vh_done)
            turns(dve, neigh_turn)
            n_low(Block(None, PT - 1))
            dve.wait_ge(v_top_made, PT)
            dve.tensor_reduce(v_top, v_tops[:, :], AX.X, ALU.max).then_inc(v_top_made, 1)
            dve.wait_ge(v_top_reduced, 1)
            power_below(v_inv, v_top)
            scale_link(dve.reciprocal(v_scale, v_inv))
            scale_link(dve.tensor_scalar(v_scale, v_scale, TOP, None, ALU.mult))
            dve.tensor_scalar(v_inv, v_inv, 1.0 / TOP, None, ALU.mult).then_inc(v_scaled, 1)
            dve.wait_ge(v_scaled, 1)

            def x_turn(turn):
                if turn.plus(1).exists:
                    copy_rows_t(turn.plus(1), PT, yz_done)
                part = bass.ds(PROLOGUE_ROWS * turn.n, PROLOGUE_ROWS)
                dve.wait_ge(v_hi_made, turn.n + 1)
                dve.scalar_tensor_tensor(out=v16[:, part, DV:2 * DV], in0=v32[:, part, :], scalar=v_scale,
                                         in1=v16[:, part, 0:DV], op0=ALU.mult,
                                         op1=ALU.subtract).then_inc(v_lo_made, 1)
                for u in range(PROLOGUE_ROWS):
                    b = PROLOGUE_ROWS * turn.n + u
                    dve.wait_ge(y_copied, b + 1)
                    dve.tensor_tensor(z[:, bass.ds(b, 1), :], ps_s[u % 2][:, D:2 * D].unsqueeze(1),
                                      z_bias[:, :].unsqueeze(1), ALU.add).then_inc(yz_read, 1)
                    dve.tensor_reduce(y_tops[:, bass.ds(b, 1)], y32[:, bass.ds(b, 1), :], AX.XY, ALU.max,
                                      apply_absolute_value=True).then_inc(y_top_made, 1)

            copy_rows_t(Block(None, 0), PT, yz_done)
            turns(dve, x_turn)
            dve.wait_ge(y_top_made, NB)
            dve.tensor_reduce(y_top, y_tops[:, :], AX.X, ALU.max).then_inc(y_top_made, 1)

            def make_bias(b, q):
                dve.wait_ge(adj_in[q], 16 * (b.n + 1))
                if b.is_first() and q == 0:
                    dve.wait_ge(v_lo_made, PT)
                    dve.wait_ge(yz_done, NB)
                src = adj_sb[:, q, :]
                if q < 2:
                    at_least(dve, mask_t_in[q], 16 * b.n)
                    dve.tensor_scalar(mask[:, q * QW:(q + 1) * QW], src, 0.0, None,
                                      ALU.is_gt).then_inc(mask_made_dve, 1)
                if q == 0:
                    at_least(dve, mask_made_act, 2 * (b.n - 1))
                dve.tensor_scalar(bias[:, b.odd, q * QW:(q + 1) * QW], src, 0.0, -BIG, ALU.is_le,
                                  ALU.mult).then_inc(bias_made, 1)

            for q in range(NQ):
                make_bias(Block(None, 0), q)
            dve.wait_ge(y_top_reduced, 1)
            power_below(y_inv, y_top)
            scale_link(dve.reciprocal(y_scale, y_inv))
            scale_link(dve.tensor_scalar(y_scale, y_scale, TOP, None, ALU.mult))
            dve.tensor_scalar(y_inv, y_inv, 1.0 / TOP, None, ALU.mult).then_inc(y_scaled, 1)
            dve.wait_ge(y_scaled, 1)
            with dve.Fori(0, PT) as i:
                part = bass.ds(PROLOGUE_ROWS * i, PROLOGUE_ROWS)
                dve.wait_ge(y_hi_made, i + 1)
                dve.scalar_tensor_tensor(out=y16[:, part, Y_LO:Y_LO + D], in0=y32[:, part, :], scalar=y_scale,
                                         in1=y16[:, part, 0:D], op0=ALU.mult,
                                         op1=ALU.subtract).then_inc(y_lo_made, 1)

            def masked_scores(t, k):
                dve.wait_ge(s_done, NG * t.n + k + 1)
                if k == 0:
                    at_least(dve, pt_done, NG * (t.n - 1))
                    at_least(dve, bias_made, NQ * (t.n + 1))
                part = slice(k * GW, (k + 1) * GW)
                apart(dve, dve_passed)
                dve.tensor_tensor_reduce(score[:, t.odd, part], ps_s[k % 2][:, :], bias[:, t.odd, part],
                                         score_scale, -3.0e38, ALU.add, ALU.max,
                                         part_max[:, k:k + 1]).then_inc(score_made, 1)

            def row_max(t):
                dve.wait_ge(score_made, NG * (t.n + 1))
                dve.tensor_reduce(row[:, 0:1], part_max[:, :], AX.X, ALU.max).then_inc(max_step, 1)
                dve.wait_ge(max_step, 4 * t.n + 1)
                dve.tensor_scalar(row[:, 1:2], row[:, 0:1], 0.0, (1 - SLOPE) / SLOPE, ALU.max,
                                  ALU.mult).then_inc(max_step, 1)
                at_least(dve, exp_made, NQ * t.n)
                dve.wait_ge(max_step, 4 * t.n + 2)
                dve.tensor_tensor(row[:, 2:3], row[:, 0:1], row[:, 1:2], ALU.add).then_inc(max_step, 1)
                dve.wait_ge(max_step, 4 * t.n + 3)
                dve.tensor_scalar(row[:, 3:4], row[:, 2:3], -1.0, EXP_SHIFT, ALU.mult, ALU.add).then_inc(max_step, 1)

            def layer0(b):
                hi, lo = ps_agg[0], ps_agg[1]
                base = 9 * b.n
                dve.wait_ge(agg_done, NQ * (b.n + 1))
                dve.tensor_scalar(row[:, 4:5], hi[:, Y_ONE:Y_ONE + 1], 1.0, None, ALU.max).then_inc(l0_step, 1)
                dve.wait_ge(l0_step, base + 1)
                dve.reciprocal(row[:, 5:6], row[:, 4:5]).then_inc(l0_step, 1)
                dve.wait_ge(l0_step, base + 2)
                dve.tensor_scalar(row[:, 6:7], row[:, 5:6], y_inv, None, ALU.mult).then_inc(l0_step, 1)
                dve.wait_ge(l0_step, base + 3)
                dve.scalar_tensor_tensor(out=l0[:, :].unsqueeze(1), in0=lo[:, 0:D].unsqueeze(1), scalar=row[:, 6:7],
                                         in1=z[:, bass.ds(b.n, 1), :],
                                         op0=ALU.mult, op1=ALU.add).then_inc(l0_step, 1)
                dve.wait_ge(l0_step, base + 4)
                dve.scalar_tensor_tensor(out=l0[:, :], in0=hi[:, 0:D], scalar=row[:, 6:7], in1=l0[:, :],
                                         op0=ALU.mult, op1=ALU.add).then_inc(l0_step, 1)
                dve.wait_ge(x_in_in[b.odd], 16 * (b.pair + 1))
                dve.wait_ge(l0_step, base + 5)
                dve.scalar_tensor_tensor(out=l0[:, :], in0=l0[:, :], scalar=0.0, in1=x_in[:, b.odd, :],
                                         op0=ALU.max, op1=ALU.add).then_inc(l0_step, 1)
                dve.wait_ge(l0_step, base + 6)
                dve.bn_stats(stat1[:, :], l0[:, :]).then_inc(l0_step, 1)
                dve.wait_ge(l0_step, base + 7)
                apart(dve, dve_passed)
                dve.bn_aggr(mv1[:, 0:2], stat1[:, :]).then_inc(l0_step, 1)
                dve.wait_ge(l0_step, base + 8)
                dve.tensor_scalar(mv1[:, 2:3], mv1[:, 1:2], LN_EPS, None, ALU.add).then_inc(l0_step, 1)

            def norm1(b):
                dve.wait_ge(rstd1_made, b.n + 1)
                at_least(dve, resx_made, b.n)
                at_least(dve, x1_t_done, b.n)
                dve.tensor_scalar(x1[:, :], l0[:, :], mv1[:, 0:1], mv1[:, 3:4], ALU.subtract,
                                  ALU.mult).then_inc(x1_made, 1)

            def xatt_low(b):
                dve.wait_ge(xatt_hi, b.n + 1)
                s = slice(2 * H, 4 * H)
                dve.scalar_tensor_tensor(out=stack[s, :], in0=ps_x[s, 0:P], scalar=bx2_sb[s, 0:1], in1=stack[s, :],
                                         op0=ALU.add, op1=ALU.subtract).then_inc(stack_ready, 1)

            def p_low(b, g):
                dve.wait_ge(p_hi_made, NG * b.n + g + 1)
                dve.tensor_tensor(p_lo[:, g % 2, :], ps_t[g % 2][:, :], p_hi[:, g % 2, :],
                                  ALU.subtract).then_inc(p_lo_made, 1)

            def add_fx(t):
                dve.wait_ge(resx_made, t.n + 1)
                dve.wait_ge(hf_done, t.n + 1)
                dve.tensor_tensor(res[:, t.odd, 0:DV], ps_x[:, 3 * P:4 * P], res[:, t.odd, 0:DV],
                                  ALU.add).then_inc(res_made, 1)

            def layer1(b):
                base = 7 * b.n
                right = res[:, b.odd, DV:D]
                dve.wait_ge(exp_made, NQ * (b.n + 1))
                dve.tensor_reduce(row2[:, 0:1], sums[:, b.odd, :], AX.X, ALU.add).then_inc(l1_step, 1)
                dve.wait_ge(l1_step, base + 1)
                dve.reciprocal(row2[:, 1:2], row2[:, 0:1]).then_inc(l1_step, 1)
                dve.wait_ge(l1_step, base + 2)
                dve.tensor_scalar(row2[:, 2:3], row2[:, 1:2], v_inv, None, ALU.mult).then_inc(l1_step, 1)
                dve.wait_ge(pv_done, NG * (b.n + 1))
                dve.wait_ge(res_made, b.n + 1)
                dve.wait_ge(l1_step, base + 3)
                dve.scalar_tensor_tensor(out=right, in0=ps_v[:, DV:2 * DV], scalar=row2[:, 2:3], in1=right,
                                         op0=ALU.mult, op1=ALU.add).then_inc(l1_step, 1)
                dve.wait_ge(l1_step, base + 4)
                dve.scalar_tensor_tensor(out=right, in0=ps_v[:, 0:DV], scalar=row2[:, 2:3], in1=right,
                                         op0=ALU.mult, op1=ALU.add).then_inc(l1_step, 1)
                dve.wait_ge(l1_step, base + 5)
                dve.bn_stats(stat2[:, :], res[:, b.odd, :]).then_inc(l1_step, 1)
                dve.wait_ge(l1_step, base + 6)
                apart(dve, dve_passed)
                dve.bn_aggr(mv2[:, 0:2], stat2[:, :]).then_inc(agg_read, 1)
                dve.wait_ge(agg_read, b.n + 1)
                dve.tensor_scalar(mv2[:, 2:3], mv2[:, 1:2], LN_EPS, None, ALU.add).then_inc(l1_step, 1)

            def norm2(b):
                dve.wait_ge(rstd2_made, b.n + 1)
                at_least(dve, out_sent, 16 * b.n)
                dve.tensor_scalar(out_sb[:, :], res[:, b.odd, :], mv2[:, 0:1], mv2[:, 3:4], ALU.subtract,
                                  ALU.mult).then_inc(out_made, 1)

            def step(t):
                enter, sink, ahead, done = t.plus(1), t.plus(-1), t.plus(2), t.plus(-2)
                for k in range(NG):
                    if t.exists:
                        masked_scores(t, k)
                    if done.exists and k == 1:
                        layer1(done)
                    if done.exists and k == 6:
                        norm2(done)
                if t.exists:
                    row_max(t)
                    add_fx(t)
                if enter.exists:
                    layer0(enter)
                for g in range(NG):
                    if ahead.exists and g in (0, 1, 2, 3) and not ahead.is_first():
                        make_bias(ahead, g)
                    if g == 1 and enter.exists:
                        norm1(enter)
                    if sink.exists:
                        p_low(sink, g)
                if enter.exists:
                    xatt_low(enter)

            walk(dve, step)

        @block.scalar
        def _(act):
            def copy_rows_t(turn, first, done):
                act.wait_ge(rows_transposed, 2 * (turn.n + first) + 1)
                at_least(act, done, PROLOGUE_ROWS * (turn.n - 1))
                act.copy(rows_t[:, turn.odd, 0, :], ps_t[0][:, :]).then_inc(rows_t_act, 1)

            def h_t_copy(turn):
                act.wait_ge(h_transposed, turn.n + 1)
                at_least(act, natt_done, turn.n)
                act.copy(h_t, ps_agg[0][0:H, :]).then_inc(h_t_copied, 1)

            def n_high(turn):
                act.wait_ge(natt_done, turn.n + 1)
                act.activation(n16[:, bass.ds(GW * turn.n, GW)], ps_agg[1][:, :], ACT.Identity,
                               bias=bn2_sb[:, 0:1]).then_inc(natt_hi, 1)

            def neigh_turn(turn):
                if turn.plus(1).exists:
                    copy_rows_t(turn.plus(1), 0, vh_done)
                if turn.plus(-1).exists:
                    h_t_copy(turn.plus(-1))
                act.wait_ge(h_made, PROLOGUE_ROWS * (turn.n + 1))
                act.activation(h_row[:, turn.odd], h_row[:, turn.odd], ACT.Tanh).then_inc(h_tanh, 1)
                if turn.plus(-1).exists:
                    n_high(turn.plus(-1))

            copy_rows_t(Block(None, 0), 0, vh_done)
            turns(act, neigh_turn)
            h_t_copy(Block(None, PT - 1))
            n_high(Block(None, PT - 1))

            def x_turn(turn):
                if turn.plus(1).exists:
                    copy_rows_t(turn.plus(1), PT, yz_done)
                part = bass.ds(PROLOGUE_ROWS * turn.n, PROLOGUE_ROWS)
                act.wait_ge(v_scaled, 1)
                act.activation(v16[:, part, 0:DV], v32[:, part, :], ACT.Copy, scale=v_scale).then_inc(v_hi_made, 1)
                for u in range(PROLOGUE_ROWS):
                    b = PROLOGUE_ROWS * turn.n + u
                    act.wait_ge(yz_done, b + 1)
                    act.copy(y32[:, bass.ds(b, 1), :], ps_s[u % 2][:, 0:D].unsqueeze(1)).then_inc(y_copied, 1)

            copy_rows_t(Block(None, 0), PT, yz_done)
            turns(act, x_turn)

            def act_mask(b, q):
                act.wait_ge(bias_made, NQ * b.n + q + 1)
                at_least(act, mask_t_in[q], 16 * b.n)
                act.activation(mask[:, q * QW:(q + 1) * QW], bias[:, b.odd, q * QW:(q + 1) * QW], ACT.Copy,
                               scale=1.0 / BIG, bias=1.0).then_inc(mask_made_act, 1)

            for q in (2, 3):
                act_mask(Block(None, 0), q)
            act.wait_ge(y_scaled, 1)
            with act.Fori(0, PT) as i:
                part = bass.ds(PROLOGUE_ROWS * i, PROLOGUE_ROWS)
                act.activation(y16[:, part, 0:D], y32[:, part, :], ACT.Copy, scale=y_scale).then_inc(y_hi_made, 1)

            def make_bend(t, q):
                act.wait_ge(score_made, NG * t.n + 2 * q + 2)
                at_least(act, leaky_made, NQ * t.n + q - 1)
                act.activation(bend[:, q % 2, :], score[:, t.odd, q * QW:(q + 1) * QW], ACT.Relu,
                               scale=(1 - SLOPE) / SLOPE).then_inc(bend_made, 1)

            def p_high(b, g):
                act.wait_ge(pt_done, NG * b.n + g + 1)
                at_least(act, pv_done, NG * b.n + g - 1)
                act.copy(p_hi[:, g % 2, :], ps_t[g % 2][:, :]).then_inc(p_hi_made, 1)

            def exps(t, q):
                act.wait_ge(max_step, 4 * (t.n + 1))
                act.wait_ge(leaky_made, NQ * t.n + q + 1)
                at_least(act, l1_step, 7 * (t.n - 2) + 1)
                part = score[:, t.odd, q * QW:(q + 1) * QW]
                act.activation(part, part, ACT.Exp, bias=row[:, 3:4],
                               accum_out=sums[:, t.odd, q:q + 1]).then_inc(exp_made, 1)

            def step(t):
                enter, sink, ahead = t.plus(1), t.plus(-1), t.plus(2)
                if t.exists:
                    for q in range(NQ):
                        make_bend(t, q)
                for g in range(NG):
                    if sink.exists:
                        p_high(sink, g)
                    if enter.exists and g == 3:
                        act.wait_ge(x1_t_done, enter.n + 1)
                        at_least(act, hf_done, enter.n)
                        act.copy(x1_t[:, :], ps_x[:, 0:D]).then_inc(x1_t_copied, 1)
                    if ahead.exists and not ahead.is_first() and g in (2, 4):
                        act_mask(ahead, 2 if g == 2 else 3)
                    if enter.exists and g == 5:
                        act.wait_ge(hf_done, enter.n + 1)
                        at_least(act, xatt_done, enter.n)
                        act.activation(tanh_sb[:, :], ps_x[0:H, 2 * P:3 * P], ACT.Tanh,
                                       bias=bx1_sb[:, 0:1]).then_inc(tanh_made, 1)
                    if t.exists and g in (5, 6):
                        exps(t, g - 5)
                if enter.exists:
                    act.wait_ge(xatt_done, enter.n + 1)
                    at_least(act, s_done, NG * enter.n)
                    act.activation(stack[:, :], ps_x[:, 0:P], ACT.Identity, bias=bx2_sb[:, 0:1]).then_inc(xatt_hi, 1)
                if t.exists:
                    exps(t, 2)
                    exps(t, 3)

            walk(act, step)

        @block.tensor
        def _(pe):
            pe.wait_ge(ident_ready, 1)
            pe.wait_ge(weights_in, 16 * len(SMALL_DMAS))
            for k, w in enumerate((ws_raw, wn_raw)):
                for kc in range(DC):
                    for dc in range(DC):
                        at = (kc * DC + dc) * P
                        mm = pe.transpose(ps_t[k][:, at:at + P], w[:, dc, kc * P:(kc + 1) * P], ident[:, :])
                mm.then_inc(w_transposed, 1)
            pe.wait_ge(w_t_copied, 2)
            for dc in range(DC):
                for w_t, c0, col in ((wn_t, DC, 0), (ws_t, 0, D)):
                    for kc in range(DC):
                        at = (kc * DC + dc) * P
                        mm = pe.matmul(ps_s[dc][:, col:col + D], w_t[:, at:at + P], wc_raw[:, c0 + kc, :],
                                       start=(kc == 0), stop=(kc == DC - 1))
                mm.then_inc(m_done, 1)
            pe.wait_ge(b_wide_made, 2 * DC)
            for c in range(2 * DC):
                mm = pe.matmul(ps_v[:, 0:D], b_wide[:, c, :], wc_raw[:, c, :], start=(c == 0), stop=(c == 2 * DC - 1))
            mm.then_inc(m_done, 1)
            pe.wait_ge(m_copied, DC + 1)

            def rows_turn(turn, first):
                pe.wait_ge(rows_in[turn.odd], 16 * (turn.pair + first // 2 + 1))
                for dc, copied in enumerate((rows_t_act, rows_t_dve)):
                    at_least(pe, copied, turn.n + first)
                    for u in range(PROLOGUE_ROWS):
                        mm = pe.transpose(ps_t[dc][:, u * P:(u + 1) * P],
                                          row_in[:, turn.odd, u, dc * P:(dc + 1) * P], ident[:, :])
                    mm.then_inc(rows_transposed, 1)

            def hidden_transposes(turn):
                pe.wait_ge(h_tanh, turn.n + 1)
                at_least(pe, h_t_copied, turn.n)
                for u in range(PROLOGUE_ROWS):
                    mm = pe.transpose(ps_agg[0][0:H, u * P:(u + 1) * P], h_row[:, turn.odd, u, :], ident[:, :])
                mm.then_inc(h_transposed, 1)

            def neigh_attention(turn):
                pe.wait_ge(h_t_copied, turn.n + 1)
                at_least(pe, natt_lo, turn.n)
                pe.matmul(ps_agg[1][:, :], wn2_sb[:, :], h_t, start=True, stop=True).then_inc(natt_done, 1)

            def neigh_turn(turn):
                if turn.plus(1).exists:
                    rows_turn(turn.plus(1), 0)
                if turn.plus(-1).exists:
                    hidden_transposes(turn.plus(-1))
                pe.wait_ge(rows_t_act, turn.n + 1)
                pe.wait_ge(rows_t_dve, turn.n + 1)
                for u in range(PROLOGUE_ROWS):
                    at_least(pe, vh_read, PROLOGUE_ROWS * turn.n + max(u - 1, 0))
                    for dc in range(DC):
                        mm = pe.matmul(ps_s[u % 2][:, 0:DV + H], rows_t[:, turn.odd, dc, u * P:(u + 1) * P],
                                       wvn[:, dc, :], start=(dc == 0), stop=(dc == DC - 1))
                    mm.then_inc(vh_done, 1)
                if turn.plus(-1).exists:
                    neigh_attention(turn.plus(-1))

            pe.wait_ge(bounds_scaled, 1)
            rows_turn(Block(None, 0), 0)
            turns(pe, neigh_turn)
            hidden_transposes(Block(None, PT - 1))
            rows_turn(Block(None, 0), PT)
            neigh_attention(Block(None, PT - 1))

            def x_turn(turn):
                if turn.plus(1).exists:
                    rows_turn(turn.plus(1), PT)
                pe.wait_ge(rows_t_act, turn.n + PT + 1)
                pe.wait_ge(rows_t_dve, turn.n + PT + 1)
                for u in range(PROLOGUE_ROWS):
                    at_least(pe, yz_read, PROLOGUE_ROWS * turn.n + max(u - 1, 0))
                    if turn.is_first():
                        pe.wait_ge(vh_read, NB)
                    for dc in range(DC):
                        mm = pe.matmul(ps_s[u % 2][:, :], rows_t[:, turn.odd, dc, u * P:(u + 1) * P],
                                       m_both[:, dc, :], start=(dc == 0), stop=(dc == DC - 1))
                    mm.then_inc(yz_done, 1)

            turns(pe, x_turn)

            def aggregate(b, c):
                if c % CQ == 0:
                    pe.wait_ge(mask_t_in[c // CQ], 16 * (b.n + 1))
                if c == 0:
                    at_least(pe, l0_step, 9 * (b.n - 1) + 5)
                if b.is_first() and c % PROLOGUE_ROWS == 0:
                    pe.wait_ge(y_lo_made, c // PROLOGUE_ROWS + 1)
                pe.matmul(ps_agg[0][:, 0:D + 1], mask_t[:, c, :], y16[:, c, 0:D + 1], start=(c == 0),
                          stop=(c == NC - 1))
                mm = pe.matmul(ps_agg[1][:, 0:D], mask_t[:, c, :], y16[:, c, Y_LO:Y_LO + D], start=(c == 0),
                               stop=(c == NC - 1))
                if c % CQ == CQ - 1:
                    mm.then_inc(agg_done, 1)

            def scores(t, k):
                if k == 0:
                    pe.wait_ge(stack_ready, t.n + 1)
                at_least(pe, score_made, NG * t.n + k - 1)
                pe.matmul(ps_s[k % 2][:, :], stack[:, :], n16[:, k * GW:(k + 1) * GW], start=True,
                          stop=True).then_inc(s_done, 1)

            def turn_p(b, g):
                if g % 2 == 0:
                    pe.wait_ge(exp_made, NQ * b.n + g // 2 + 1)
                at_least(pe, p_lo_made, NG * b.n + g - 1)
                for u in range(CG):
                    at = g * GW + u * P
                    mm = pe.transpose(ps_t[g % 2][:, u * P:(u + 1) * P], score[:, b.odd, at:at + P], ident[:, :])
                mm.then_inc(pt_done, 1)

            def weigh_values(b, g):
                pe.wait_ge(p_lo_made, NG * b.n + g + 1)
                if g == 0:
                    at_least(pe, l1_step, 7 * (b.n - 1) + 5)
                for u in range(CG):
                    c = g * CG + u
                    chunk = slice(u * P, (u + 1) * P)
                    for part in (("hi", "lo") if c == 0 else ("lo", "hi")):
                        if part == "hi":
                            mm = pe.matmul(ps_v[:, 0:2 * DV], p_hi[:, g % 2, chunk], v16[:, c, :], start=(c == 0),
                                           stop=(c == NC - 1), skip_group_check=True)
                        else:
                            mm = pe.matmul(ps_v[:, DV:2 * DV], p_lo[:, g % 2, chunk], v16[:, c, 0:DV],
                                           start=False, stop=False, skip_group_check=True)
                mm.then_inc(pv_done, 1)

            def x1_transpose(b):
                pe.wait_ge(x1_made, b.n + 1)
                at_least(pe, stack_ready, b.n)
                at_least(pe, res_made, b.n)
                for dc in range(DC):
                    mm = pe.transpose(ps_x[:, dc * P:(dc + 1) * P], x1[:, dc * P:(dc + 1) * P], ident[:, :])
                mm.then_inc(x1_t_done, 1)

            def hidden_and_fx(b):
                pe.wait_ge(x1_t_copied, b.n + 1)
                for dc in range(DC):
                    pe.matmul(ps_x[0:H, 2 * P:3 * P], wx1_sb[:, dc, :], x1_t[:, dc * P:(dc + 1) * P],
                              start=(dc == 0), stop=(dc == DC - 1))
                for dc in range(DC):
                    mm = pe.matmul(ps_x[:, 3 * P:4 * P], x1_t[:, dc * P:(dc + 1) * P], wfx_sb[:, dc, :],
                                   start=(dc == 0), stop=(dc == DC - 1))
                mm.then_inc(hf_done, 1)

            def x_attention(b):
                pe.wait_ge(tanh_made, b.n + 1)
                pe.matmul(ps_x[:, 0:P], wx2_sb[:, :], tanh_sb[:, :], start=True, stop=True).then_inc(xatt_done, 1)

            def step(t):
                enter, sink = t.plus(1), t.plus(-1)
                for c in range(NC):
                    if enter.exists:
                        aggregate(enter, c)
                    if t.exists and c % CG == CG - 1:
                        scores(t, c // CG)
                for g in range(NG + 2):
                    if sink.exists and g < NG:
                        turn_p(sink, g)
                    if sink.exists and g >= 2:
                        weigh_values(sink, g - 2)
                    if enter.exists and g == 3:
                        x1_transpose(enter)
                    if enter.exists and g == 5:
                        hidden_and_fx(enter)
                    if enter.exists and g == 7:
                        x_attention(enter)

            walk(pe, step)


_INS = ['x', 'adj', 'L0_gnn_W_self', 'L0_gnn_b_self', 'L0_gnn_W_nb', 'L0_gnn_b_nb', 'L0_gnn_W_comb', 'L0_gnn_b_comb',
        'L1_gnn_neigh', 'L1_gnn_Wx1', 'L1_gnn_bx1', 'L1_gnn_Wx2', 'L1_gnn_bx2', 'L1_gnn_Wn1', 'L1_gnn_bn1',
        'L1_gnn_Wn2', 'L1_gnn_bn2', 'L1_gnn_Wv', 'L1_gnn_bv', 'L1_gnn_Wfx', 'L1_gnn_bfx']


def kernel(**inputs):
    import numpy as _np
    import concourse.bacc as _bacc
    from concourse import mybir as _mybir
    from concourse.bass_utils import run_bass_kernel_spmd as _run

    nc = _bacc.Bacc("TRN2", target_bir_lowering=False, num_devices=1)
    arrays, args = {}, []
    for name in _INS:
        a = _np.ascontiguousarray(inputs[name])
        arrays[f"in_{name}_dram"] = a
        args.append(nc.dram_tensor(f"in_{name}_dram", a.shape, _mybir.dt.from_np(a.dtype), kind="ExternalInput").ap())
    out = nc.dram_tensor("out_dram", (N, D), _mybir.dt.float32, kind="ExternalOutput").ap()
    gnn_kernel(nc, *args, out)
    r = _run(nc, [arrays], core_ids=[0])
    return r.results[0]["out_dram"]
```
